# Optimizing a Trainium2 kernel written in Bass

```python
import numpy as np
import jax
import jax.numpy as jnp

def _softmax(x, axis=-1):
    return jax.nn.softmax(x, axis=axis)

def _gelu(x):
    return jax.nn.gelu(x, approximate=True)

def _silu(x):
    return jax.nn.silu(x)

def _sigmoid(x):
    return jax.nn.sigmoid(x)

def _layernorm(x, axis=-1, eps=1e-05):
    m = jnp.mean(x, axis=axis, keepdims=True)
    v = jnp.var(x, axis=axis, keepdims=True)
    return (x - m) / jnp.sqrt(v + eps)

def _scatter_add(tgt, idx, src, axis=0):
    return tgt.at[idx].add(src)

def _segment_sum(src, seg, n):
    return jax.ops.segment_sum(src, seg, n)
kernel_name = 'mk_gnn_resnorm_d2_gnn_r8_a575fa'

def setup_inputs(seed: int=0):
    np.random.seed(seed)
    _w = jnp.asarray

    def _rec_inputs():
        import jax
        import jax.numpy as jnp
        _gk = jax.random.key(seed)
        x = -0.0003713 + 1 * jax.random.normal(jax.random.fold_in(_gk, 1), (12500, 128), jnp.float32)
        src = jax.random.randint(jax.random.fold_in(_gk, 2), (200000,), 0, 12500, jnp.int32)
        dst = jax.random.randint(jax.random.fold_in(_gk, 3), (200000,), 0, 12500, jnp.int32)
        _o = jnp.argsort(dst, stable=True)
        src = src[_o]
        dst = dst[_o]
        edge_attr_64 = 0.000189758 + 1.00013 * jax.random.normal(jax.random.fold_in(_gk, 12), (200000, 64), jnp.float32)
        return (x, src, dst, edge_attr_64)
    x, src, dst, edge_attr_64 = _rec_inputs()

    def _L0_gnn_setup():
        import jax, jax.numpy as jnp
        import numpy as np
        N_NODES = 12500
        key = jax.random.key(seed)
        k1, k2, k3 = jax.random.split(key, 3)
        x = jax.random.normal(k1, (N_NODES, 128), dtype=jnp.float32)
        src_idx = jax.random.randint(k2, (250000,), 0, N_NODES, dtype=jnp.int64)
        dst_idx = jax.random.randint(k3, (250000,), 0, N_NODES, dtype=jnp.int64)
        return {'x': x, 'src_idx': src_idx, 'dst_idx': dst_idx}
    _L0_gnn_all = _L0_gnn_setup()
    _L0_gnn_in = {k: v for k, v in _L0_gnn_all.items() if k in ()}
    del _L0_gnn_all

    def _L1_gnn_setup():
        import jax, jax.numpy as jnp
        import numpy as np
        N, E, D, H, ED = (6250, 100000, 128, 8, 64)
        C = D // H

        def _ln(x, g, b, eps=1e-05):
            m = jnp.mean(x, axis=-1, keepdims=True)
            v = jnp.var(x, axis=-1, keepdims=True)
            return (x - m) * jax.lax.rsqrt(v + eps) * g + b
        key = jax.random.key(seed)
        ks = jax.random.split(key, 16)
        p = lambda k, shape: jax.random.normal(k, shape, dtype=jnp.float32) * 0.05
        return {'x': jax.random.normal(ks[0], (N, D), dtype=jnp.float32), 'edge_index': jax.random.randint(ks[1], (2, E), 0, N, dtype=jnp.int64), 'edge_attr': jax.random.normal(ks[2], (E, ED), dtype=jnp.float32), 'Wq': p(ks[3], (D, D)), 'bq': jnp.zeros((D,), jnp.float32), 'Wk': p(ks[4], (D, D)), 'bk': jnp.zeros((D,), jnp.float32), 'Wv': p(ks[5], (D, D)), 'bv': jnp.zeros((D,), jnp.float32), 'We': p(ks[6], (ED, D)), 'Wskip': p(ks[7], (D, D)), 'bskip': jnp.zeros((D,), jnp.float32), 'g1': jnp.ones((D,), jnp.float32), 'b1': jnp.zeros((D,), jnp.float32), 'g2': jnp.ones((D,), jnp.float32), 'b2': jnp.zeros((D,), jnp.float32), 'Wf1': p(ks[8], (D, 4 * D)), 'bf1': jnp.zeros((4 * D,), jnp.float32), 'Wf2': p(ks[9], (4 * D, D)), 'bf2': jnp.zeros((D,), jnp.float32)}
    _L1_gnn_all = _L1_gnn_setup()
    _L1_gnn_in = {k: v for k, v in _L1_gnn_all.items() if k in ('Wq', 'bq', 'Wk', 'bk', 'Wv', 'bv', 'We', 'Wskip', 'bskip', 'g1', 'b1', 'g2', 'b2', 'Wf1', 'bf1', 'Wf2', 'bf2')}
    del _L1_gnn_all
    return {'x': x, 'src': src, 'dst': dst, 'edge_attr_64': edge_attr_64, 'L1_gnn_Wq': _L1_gnn_in['Wq'], 'L1_gnn_bq': _L1_gnn_in['bq'], 'L1_gnn_Wk': _L1_gnn_in['Wk'], 'L1_gnn_bk': _L1_gnn_in['bk'], 'L1_gnn_Wv': _L1_gnn_in['Wv'], 'L1_gnn_bv': _L1_gnn_in['bv'], 'L1_gnn_We': _L1_gnn_in['We'], 'L1_gnn_Wskip': _L1_gnn_in['Wskip'], 'L1_gnn_bskip': _L1_gnn_in['bskip'], 'L1_gnn_g1': _L1_gnn_in['g1'], 'L1_gnn_b1': _L1_gnn_in['b1'], 'L1_gnn_g2': _L1_gnn_in['g2'], 'L1_gnn_b2': _L1_gnn_in['b2'], 'L1_gnn_Wf1': _L1_gnn_in['Wf1'], 'L1_gnn_bf1': _L1_gnn_in['bf1'], 'L1_gnn_Wf2': _L1_gnn_in['Wf2'], 'L1_gnn_bf2': _L1_gnn_in['bf2']}

def reference(x, src, dst, edge_attr_64, L1_gnn_Wq, L1_gnn_bq, L1_gnn_Wk, L1_gnn_bk, L1_gnn_Wv, L1_gnn_bv, L1_gnn_We, L1_gnn_Wskip, L1_gnn_bskip, L1_gnn_g1, L1_gnn_b1, L1_gnn_g2, L1_gnn_b2, L1_gnn_Wf1, L1_gnn_bf1, L1_gnn_Wf2, L1_gnn_bf2):
    import jax
    import jax.numpy as jnp

    def _L0_gnn_ref(x, src_idx, dst_idx):
        import jax, jax.numpy as jnp
        import numpy as np
        N_NODES = 12500
        x_j = x[src_idx]
        agg = jax.ops.segment_sum(x_j, dst_idx, num_segments=x.shape[0])
        return x + agg

    def _L1_gnn_ref(x, edge_index, edge_attr, Wq, bq, Wk, bk, Wv, bv, We, Wskip, bskip, g1, b1, g2, b2, Wf1, bf1, Wf2, bf2):
        import jax, jax.numpy as jnp
        import numpy as np
        N, E, D, H, ED = (6250, 100000, 128, 8, 64)
        C = D // H

        def _ln(x, g, b, eps=1e-05):
            m = jnp.mean(x, axis=-1, keepdims=True)
            v = jnp.var(x, axis=-1, keepdims=True)
            return (x - m) * jax.lax.rsqrt(v + eps) * g + b
        n = x.shape[0]
        src, dst = (edge_index[0], edge_index[1])
        q = (x @ Wq + bq).reshape(n, H, C)
        k = (x @ Wk + bk).reshape(n, H, C)
        v = (x @ Wv + bv).reshape(n, H, C)
        e = (edge_attr @ We).reshape(-1, H, C)
        k_j = k[src] + e
        v_j = v[src] + e
        logits = jnp.sum(q[dst] * k_j, axis=-1) / np.sqrt(C)
        m = jax.ops.segment_max(logits, dst, num_segments=n)
        ex = jnp.exp(logits - m[dst])
        denom = jax.ops.segment_sum(ex, dst, num_segments=n)
        alpha = ex / denom[dst]
        agg = jax.ops.segment_sum(alpha[..., None] * v_j, dst, num_segments=n)
        conv = agg.reshape(n, D) + x @ Wskip + bskip
        h = _ln(conv + x, g1, b1)
        ffn = jax.nn.gelu(h @ Wf1 + bf1, approximate=False) @ Wf2 + bf2
        return _ln(ffn + h, g2, b2)
    edge_index = jnp.stack([src, dst])
    x = _layernorm(x + _L0_gnn_ref(x, src, dst), axis=-1)
    x = _layernorm(x + _L1_gnn_ref(x, edge_index, edge_attr_64, L1_gnn_Wq, L1_gnn_bq, L1_gnn_Wk, L1_gnn_bk, L1_gnn_Wv, L1_gnn_bv, L1_gnn_We, L1_gnn_Wskip, L1_gnn_bskip, L1_gnn_g1, L1_gnn_b1, L1_gnn_g2, L1_gnn_b2, L1_gnn_Wf1, L1_gnn_bf1, L1_gnn_Wf2, L1_gnn_bf2), axis=-1)
    return x

_drawn_inputs = setup_inputs


def setup_inputs(seed=0):
    import zlib

    import numpy as np

    out = dict(_drawn_inputs(seed))
    spreads = {'L1_gnn_bq': (0.0, 0.8),
     'L1_gnn_bk': (0.0, 0.8),
     'L1_gnn_bv': (0.0, 0.1),
     'L1_gnn_bskip': (0.0, 0.1),
     'L1_gnn_g1': (1.0, 0.2),
     'L1_gnn_b1': (0.0, 0.1),
     'L1_gnn_g2': (1.0, 0.2),
     'L1_gnn_b2': (0.0, 0.1),
     'L1_gnn_bf1': (0.0, 0.1),
     'L1_gnn_bf2': (0.0, 0.1)}
    factors = {}
    for name, (base, spread) in spreads.items():
        noise = np.random.default_rng([zlib.crc32(name.encode()), seed]).standard_normal(out[name].shape)
        drawn = base * np.exp(spread * noise) if base else spread * noise
        out[name] = jnp.asarray(drawn.astype(out[name].dtype))
    for name, factor in factors.items():
        out[name] = (out[name] * factor).astype(out[name].dtype)
    return out
```

```python
import concourse.bass as bass
from concourse import mybir
from contextlib import ExitStack

f32 = mybir.dt.float32
bf16 = mybir.dt.bfloat16
i32 = mybir.dt.int32
i16 = mybir.dt.int16
ALU = mybir.AluOpType
ACT = mybir.ActivationFunctionType
AX = mybir.AxisListType

P = 128
N, E, D, H, ED = 12500, 200000, 128, 8, 64
C = D // H
HID = 4 * D
T = -(-N // P)
NPAD = T * P
CH = 4
BE = CH * P
NB = -(-(E + 1) // BE)
EPAD = NB * BE
STEPS = NB + T - 1
TAB = 512
R = 4
AW = H * (C + 1)
BLK = 32
NBLK = P // BLK
BIG = float(2.0 ** 100)
EPS = 1e-5
MG = 7
assert STEPS % R == 0 and STEPS <= TAB and T % MG == 0 and T % 2 == 0


def build(nc, x, srcl, dstrow, dstt, dste, dstn, lastd, attrt, wall, ball, we, wf1, wf2, rows, bf1, out):
    dsc = nc.dram_tensor("dst16_scratch", (P, EPAD // P), i16).ap()
    tabd = nc.dram_tensor("tab_scratch", (4, TAB), i32).ap()
    kvd = nc.dram_tensor("kv_scratch", (NPAD, 2 * D), f32).ap()
    h0d = nc.dram_tensor("h0_scratch", (NPAD, D), f32).ap()
    resd = nc.dram_tensor("res_scratch", (NPAD, D), f32).ap()
    dflat = dsc.rearrange("p n -> (p n)")
    ctx = ExitStack()
    sb = lambda n, s, d: ctx.enter_context(nc.sbuf_tensor(n, s, d))
    ps = lambda n, s, d: ctx.enter_context(nc.psum_tensor(n, s, d))
    sem = lambda n: ctx.enter_context(nc.semaphore(n))
    with ctx:
        big1 = sb("big1", [P, T * AW], f32)
        agg0 = big1[:, 0:T * D].rearrange("p (t d) -> p t d", d=D)
        agg1 = big1[:, :].rearrange("p (t a) -> p t a", a=AW)
        QW = 3 * D // 2
        big2 = sb("big2", [P, T * QW], f32)
        FMW = 26 * STEPS
        dT = big2[:, 0:FMW + 1].bitcast(i32)
        q3 = big2[:, :].bitcast(bf16).rearrange("p (t w) -> p t w", w=3 * D)
        Y = big2[:, 0:T * D].rearrange("p (t d) -> p t d", d=D)
        ring = sb("ring", [P, R * CH * 2 * D], f32)
        kv = ring[:, :].rearrange("p (s c w) -> p s c w", s=R, c=CH)
        xg = ring[:, 0:R * CH * D].rearrange("p (s c d) -> p s c d", s=R, c=CH)
        prep = big2[:, FMW + 11:]
        fm = sb("fm", [P, FMW + 2], bf16)
        srcs = sb("srcs", [P, NB * CH], i32)
        islast = sb("islast", [P, NB * CH], bf16)
        idx = sb("idx", [P, 2 * R, CH], i32)
        dstb = sb("dstb", [P, R, BE], i16)
        ST = sb("ST", [P, 2, BE], bf16)
        Sb = sb("Sb", [P, 2, BE], bf16)
        S32 = sb("S32", [P, 2, BE], f32)
        work = sb("work", [P, 512 + CH * AW], f32)
        prod = work[:, 0:512]
        wvx = work[:, 512:].rearrange("p (c h j) -> p c h j", c=CH, h=H)
        attrs = sb("attrs", [P, 3 * TAB], f32)
        attr = attrs[0:ED, 0:BE]
        tabs = attrs[:, :].bitcast(i32)
        tab = [tabs[ED:ED + 1, i * TAB:(i + 1) * TAB] for i in range(3)]
        rel = attrs[96:97, 0:NB + R].bitcast(i32)
        ends = attrs[96:97, TAB:TAB + NB].bitcast(i32)
        lg = sb("lg", [P, 2, CH * H], f32)
        sc4 = sb("sc4", [P, 6, CH * H], f32)
        mp = sb("mp", [P, 2, CH * H], bf16)
        Z = sb("Z", [P, 2, CH, NBLK, H], bf16)
        pz = sb("pz", [P, CH, NBLK], bf16)
        blk = sb("blk", [P, NBLK], bf16)
        blkbig = sb("blkbig", [P, NBLK], bf16)
        neg = sb("neg", [P, P], bf16)
        ones = sb("ones", [P, P], bf16)
        ident = sb("ident", [P, P], bf16)
        identf = sb("identf", [P, P], f32)
        Mr = sb("Mr", [P, T, H], f32)
        mx = sb("mx", [P, H], f32)
        nw = sb("nw", [P, H], f32)
        rp = sb("rp", [P, 2, H], bf16)
        dl = sb("dl", [P, 2, H], f32)
        scl = sb("scl", [P, 2, H], f32)
        dd = sb("dd", [P, CH * H], f32)
        tbase = sb("tbase", [P, T], f32)
        we_s = sb("we_s", [ED, D], f32)
        epsc = sb("epsc", [P, 1], f32)
        endb = sb("endb", [P, NBLK], f32)
        endc = sb("endc", [P, 1], f32)
        lnv = sb("lnv", [P, 3, T], f32)
        st = S32[:, :, :].rearrange("p a b -> p (a b)")[:, 0:T * 6].rearrange("p (t k) -> p t k", k=6)
        qs = [ring[:, k * 512:(k + 1) * 512] for k in range(2)]
        rs = [ring[:, 1024 + k * D:1024 + (k + 1) * D] for k in range(2)]
        hT = [ring[:, 1280 + k * D:1280 + (k + 1) * D] for k in range(2)]
        rr = ring[:, 1536:1536 + D]
        h0s = [ring[:, 1664 + k * D:1664 + (k + 1) * D] for k in range(2)]
        wall_s, ball_s = ring[:, 2048:2560], ring[:, 2560:3072]
        fmf = fm[:, 0:FMW].bitcast(f32)
        wf1_s, wf2_s, rows_s, bf1_s = fmf[:, 0:HID], fmf[:, HID:2 * HID], fmf[:, 2 * HID:2 * HID + 5 * D], fmf[:, 1664:1668]
        g1_s, b1_s, g2_s, b2_s, bf2_s = [rows_s[:, i * D:(i + 1) * D] for i in range(5)]
        hT2 = [fmf[:, 1700 + k * 2 * D:1700 + (k + 1) * 2 * D] for k in range(2)]
        gT = [fmf[:, 2212 + k * 4 * 2 * D:2212 + (k + 1) * 4 * 2 * D].rearrange("p (c n) -> p c n", c=4) for k in range(2)]
        hs = [fmf[:, 4260 + k * 2 * D:4260 + (k + 1) * 2 * D].rearrange("p (t d) -> p t d", d=D) for k in range(2)]
        GW = MG * D
        resb = [ring[:, k * GW:(k + 1) * GW] for k in range(2)]
        h0b = [ring[:, (2 + k) * GW:(3 + k) * GW] for k in range(2)]
        rd = work[:, 0:T * H].rearrange("p (t h) -> p t h", h=H)
        d32 = prep[:, 0:EPAD // P].bitcast(i32)
        d16 = prep[:, 1600:1600 + EPAD // P // 2].bitcast(i16)
        dE = prep[:, 2400:2400 + NB * CH].bitcast(i32)
        last = S32[:, 0, 0:NB].bitcast(i32)
        key = S32[:, 1, 0:NB]
        cmpk = prod[:, 0:NB]
        kiota = work[:, 512:512 + NB]
        scol = sc4[:, 0, 0:8]
        cnt = sc4[:, 1, 0:8]
        tabc = sc4[:, 2, 0:16].bitcast(i32).rearrange("p (k j) -> p k j", k=4)
        dN = prep[:, 0:NB * CH].bitcast(i32)
        bank = [ps(f"bank{i}", [P, 512], f32) for i in range(8)]
        psE, psZ, psR = bank[0], bank[1], bank[2]
        psS = bank[3][:, 0:256].bitcast(bf16)
        psQ = [bank[4], bank[5]]
        psA = [bank[6], bank[7]]

        psT = [bank[0], bank[1]]
        psW = [bank[2], bank[3]]
        psT2 = [bank[0], bank[1]]
        psF1 = [[bank[2], bank[3]], [bank[4], bank[5]]]
        psF2 = [bank[6], bank[7]]

        in_src = sem("in_src"); in_small = sem("in_small"); in_x = sem("in_x"); in_dt = sem("in_dt"); in_dn = sem("in_dn")
        in_w = sem("in_w")
        consts = sem("consts"); d16_done = sem("d16_done"); dsc_stored = sem("dsc_stored")
        tab_made = sem("tab_made"); tab_stored = sem("tab_stored"); tab_loaded = sem("tab_loaded")
        twice_x = sem("twice_x")
        own = sem("own")
        pace = sem("pace")
        a_dload = [sem(f"a_dload{i}") for i in range(R)]
        a_gat = [sem(f"a_gat{i}") for i in range(R)]
        a_dst = sem("a_dst"); a_x = sem("a_x"); a_free = sem("a_free"); a_idx = sem("a_idx")
        a_cmp = sem("a_cmp"); a_tr = sem("a_tr"); a_s32 = sem("a_s32"); a_agg = sem("a_agg"); a_acc = sem("a_acc")

        in_b = sem("in_b"); ln_var = sem("ln_var"); ln_std = sem("ln_std"); ln_done = sem("ln_done")
        b_h0 = sem("b_h0"); b_tr = sem("b_tr"); b_ht = sem("b_ht"); b_mm = sem("b_mm"); b_qs = sem("b_qs"); b_res = sem("b_res"); b_q3 = sem("b_q3")
        b_kvst = [sem(f"b_kvst{k}") for k in range(2)]
        b_resst = [sem(f"b_resst{k}") for k in range(2)]
        b_h0st = [sem(f"b_h0st{k}") for k in range(2)]
        c_dload = [sem(f"c_dload{i}") for i in range(R)]
        c_gat = [sem(f"c_gat{i}") for i in range(R)]
        c_aload = sem("c_aload")
        c_dst = sem("c_dst"); c_kv = sem("c_kv"); c_attr = sem("c_attr"); c_e = sem("c_e"); c_ecopy = sem("c_ecopy"); c_idx = sem("c_idx")
        c_cmp = sem("c_cmp"); c_tr = sem("c_tr"); c_sb = sem("c_sb"); c_s32 = sem("c_s32"); c_q = sem("c_q"); c_z = sem("c_z"); c_zmm = sem("c_zmm")
        c_r = sem("c_r"); c_dl = sem("c_dl"); c_rexp = sem("c_rexp"); c_d = sem("c_d"); c_ex = sem("c_ex"); c_sc = sem("c_sc")
        c_wv = sem("c_wv"); c_agg = sem("c_agg"); c_acc = sem("c_acc")
        in_d = sem("in_d"); d_res = [sem(f"d_res{k}") for k in range(2)]; d_h0 = [sem(f"d_h0{k}") for k in range(2)]
        d_y = sem("d_y"); d_hn = sem("d_hn"); d_h = sem("d_h"); d_tr = sem("d_tr"); d_ht = sem("d_ht"); d_f1 = sem("d_f1"); d_g = sem("d_g"); d_f2 = sem("d_f2")
        d_y2 = sem("d_y2"); d_n2 = sem("d_n2"); d_u = sem("d_u"); d_o = sem("d_o"); d_out = sem("d_out")

        def entries(eng, what, s, n):
            top = (NB - 1, T - 1, 1)[what]
            _, v = nc.values_load_multi_w_load_instructions(tab[what][:, bass.ds(s, n)], engines=[eng.engine],
                                                            min_val=0, max_val=top)
            return v

        def rowv(a, i):
            return a[:, bass.ds(i, 1), :].rearrange("p a d -> p (a d)")

        def hold(eng, s, v):
            eng.wait_ge(s, v)
            eng.sem_inc(pace, 1)

        def load_dst(sp, b, k, sems):
            sp.dma_start(dstb[:, k, :], dflat[bass.ds(b * BE, BE)].unsqueeze(0).broadcast_to([P, BE])).then_inc(sems[k], 16)

        def flat(a):
            return a.rearrange("p a d -> p (a d)")

        with nc.Block() as block:
            @block.sync
            def _(sp):
                sp.dma_start(last, lastd.broadcast_to([P, NB])).then_inc(in_small, 16)
                sp.dma_start(d32, dstrow).then_inc(in_small, 16)
                sp.dma_start(srcs[:, :], srcl).then_inc(in_src, 16)
                sp.wait_ge(d16_done, 1)
                sp.dma_start(dsc, d16).then_inc(dsc_stored, 16)
                sp.wait_ge(tab_made, 7)
                sp.dma_start(tabd.rearrange("k (p j) -> p k j", p=P), tabc).then_inc(tab_stored, 16)
                sp.dma_start(dE, dste).then_inc(in_dn, 16)
                sp.dma_start(dN, dstn).then_inc(in_dn, 16)
                sp.wait_ge(tab_stored, 16)
                for i in range(3):
                    sp.dma_start(tab[i], tabd[i:i + 1, :]).then_inc(tab_loaded, 16)
                sp.wait_ge(dsc_stored, 16)
                for b in range(R):
                    load_dst(sp, b, b, a_dload)
                sp.dma_start(agg0, x.rearrange("(t p) d -> p t d", p=P)).then_inc(in_x, 16)
                sp.dma_start(dT, dstt).then_inc(in_dt, 16)
                sp.dma_start(wall_s, wall).then_inc(in_b, 16)
                sp.dma_start(ball_s, ball.broadcast_to([P, 4 * D])).then_inc(in_b, 16)
                sp.dma_start(we_s[:, :], we).then_inc(in_b, 16)
                sp.dma_start(attr, attrt[:, 0:BE]).then_inc(c_aload, 16)
                for b in range(2):
                    sp.wait_ge(a_dload[b], 16)
                    sp.sem_inc(a_dst, 1)
                sp.wait_ge(tab_loaded, 48)

                def turn(b, k, g):
                    free = sp.value_load(ends[0:1, bass.ds(b, 1)], min_val=1, max_val=STEPS + 1)
                    sp.wait_ge(a_dload[(k + 2) % R], (g + (k + 2) // R) * 16 + 16)
                    sp.sem_inc(a_dst, 1)
                    sp.wait_ge(a_gat[k], g * 16 * CH + 16 * CH)
                    sp.sem_inc(a_x, 1)
                    sp.wait_ge(a_agg, free)
                    sp.sem_inc(a_free, 1)
                    load_dst(sp, b + R, k, a_dload)
                full = (NB - R) // R
                with sp.Fori(0, full) as g:
                    for k in range(R):
                        turn(g * R + k, k, g)
                for b in range(full * R, NB):
                    if b + R < NB:
                        turn(b, b % R, b // R)
                    else:
                        if b + 2 < NB:
                            sp.wait_ge(a_dload[(b + 2) % R], (b + 2) // R * 16 + 16)
                            sp.sem_inc(a_dst, 1)
                        sp.wait_ge(a_gat[b % R], (b // R + 1) * 16 * CH)
                        sp.sem_inc(a_x, 1)

                def stores(t, k):
                    rows_ = bass.ds(t * P, P)
                    hold(sp, b_h0, t + 1)
                    sp.dma_start(h0d[rows_, :], h0s[k]).then_inc(b_h0st[k], 16)
                    hold(sp, b_qs, t + 1)
                    sp.dma_start(kvd[rows_, :], qs[k][:, D:3 * D]).then_inc(b_kvst[k], 16)
                    hold(sp, b_res, t + 1)
                    sp.dma_start(resd[rows_, :], rs[k]).then_inc(b_resst[k], 16)
                with sp.Fori(0, T // 2) as g:
                    for k in range(2):
                        stores(g * 2 + k, k)

                def turn1(j, k, g, lo=False):
                    if not lo or j >= 3:
                        if not lo or j - 3 < NB:
                            sp.wait_ge(c_gat[(k + 1) % R], (g + (k + 1) // R) * 16 * CH)
                            sp.sem_inc(c_kv, 1)
                    if not lo or 2 <= j < NB + 2:
                        sp.wait_ge(c_dload[(k + 2) % R], (g + (k + 2) // R) * 16)
                        sp.sem_inc(c_dst, 1)
                    if not lo or j < NB:
                        sp.wait_ge(c_aload, j * 16 + 16)
                        sp.sem_inc(c_attr, 1)
                    if not lo or j + 1 < NB:
                        hold(sp, c_e, j + 1)
                        sp.dma_start(attr, attrt[:, bass.ds((j + 1) * BE, BE)]).then_inc(c_aload, 16)
                    if not lo or j + 1 < NB:
                        if not lo or j >= 3:
                            free = sp.value_load(ends[0:1, bass.ds(j - 3, 1)], min_val=1, max_val=STEPS + 1)
                            hold(sp, c_cmp, free)
                        load_dst(sp, j + 1, (k + 1) % R, c_dload)
                sp.wait_ge(a_cmp, STEPS)
                load_dst(sp, 0, 0, c_dload)
                for j in range(R):
                    turn1(j, j, 0, True)
                with sp.Fori(1, (NB - 2) // R) as g:
                    for k in range(R):
                        turn1(g * R + k, k, g)
                for j in range((NB - 2) // R * R, NB + 3):
                    turn1(j, j % R, j // R, True)

                sp.wait_ge(c_acc, STEPS)
                sp.dma_start(wf1_s, wf1).then_inc(in_d, 16)
                sp.dma_start(wf2_s.rearrange("p (c n) -> p c n", c=4), wf2.rearrange("(c p) n -> p c n", p=P)).then_inc(in_d, 16)
                sp.dma_start(rows_s, rows.broadcast_to([P, 5 * D])).then_inc(in_d, 16)
                sp.dma_start(bf1_s, bf1).then_inc(in_d, 16)
                dview = lambda a, m: a[bass.ds(m * MG * P, MG * P), :].rearrange("(t p) d -> p t d", p=P)
                gview = lambda a: a.rearrange("p (t d) -> p t d", d=D)
                for m in range(2):
                    sp.dma_start(gview(resb[m]), dview(resd, m)).then_inc(d_res[m], 16)
                with sp.Fori(1, T // MG // 2) as g:
                    for k in range(2):
                        hold(sp, d_y, (g * 2 + k) - 1)
                        sp.dma_start(gview(resb[k]), dview(resd, g * 2 + k)).then_inc(d_res[k], 16)
                for m in range(2):
                    sp.dma_start(gview(h0b[m]), dview(h0d, m)).then_inc(d_h0[m], 16)
                with sp.Fori(1, T // MG // 2) as g:
                    for k in range(2):
                        hold(sp, d_u, (g * 2 + k) - 1)
                        sp.dma_start(gview(h0b[k]), dview(h0d, g * 2 + k)).then_inc(d_h0[k], 16)
                with sp.Fori(0, T // MG) as m:
                    hold(sp, d_o, m + 1)
                    sp.dma_start(dview(out, m), Y[:, bass.ds(m * MG, MG), :]).then_inc(d_out, 16)
                sp.wait_ge(d_out, 16 * (T // MG))

            @block.gpsimd
            def _(pool):
                io = dict(allow_small_or_imprecise_dtypes=True)
                pool.iota(kiota, [[1, NB]], base=0, channel_multiplier=0, **io).then_inc(consts, 1)
                pool.iota(scol[:, 0:4], [[1, 4]], base=0, channel_multiplier=4, **io).then_inc(consts, 1)
                pool.iota(scol[:, 4:8], [[1, 4]], base=-1, channel_multiplier=4, **io).then_inc(consts, 1)
                pool.iota(tbase[:, :], [[P, T]], base=0, channel_multiplier=1, **io).then_inc(consts, 1)
                pool.memset(ident[:, :], 0.0).then_inc(consts, 1)
                pool.memset(identf[:, :], 0.0).then_inc(consts, 1)
                pool.memset(neg[:, :], 0.0).then_inc(consts, 1)
                pool.memset(blk[:, :], 1.0).then_inc(consts, 1)
                pool.memset(ones[:, :], 1.0).then_inc(consts, 1)
                pool.memset(epsc[:, :], EPS).then_inc(consts, 1)
                pool.memset(endb[:, :], 0.0).then_inc(consts, 1)
                pool.wait_ge(consts, 11)
                for m in (ident, identf):
                    pool.affine_select(out=m[:, :], in_=m[:, :], compare_op=ALU.not_equal, fill=1.0, base=0,
                                       pattern=[[-1, P]], channel_multiplier=1).then_inc(consts, 1)
                pool.affine_select(out=neg[:, :], in_=neg[:, :], compare_op=ALU.is_gt, fill=-BIG, base=0,
                                   pattern=[[0, P]], channel_multiplier=1).then_inc(consts, 1)
                pool.affine_select(out=endb[:, :], in_=endb[:, :], compare_op=ALU.not_equal, fill=1.0, base=1 - BLK,
                                   pattern=[[-BLK, NBLK]], channel_multiplier=1).then_inc(consts, 1)
                pool.affine_select(out=blk[:, :], in_=blk[:, :], compare_op=ALU.is_ge, fill=0.0, base=0,
                                   pattern=[[-BLK, NBLK]], channel_multiplier=1).then_inc(consts, 1)
                pool.wait_ge(consts, 16)
                pool.affine_select(out=blk[:, :], in_=blk[:, :], compare_op=ALU.is_ge, fill=0.0, base=BLK - 1,
                                   pattern=[[BLK, NBLK]], channel_multiplier=-1).then_inc(consts, 1)
                pool.wait_ge(in_src, 16)

                def edge_rows(copied, gathered, one_batch, ready):
                    def copy_idx(b, k8):
                        pool.tensor_copy(idx[:, k8, :], srcs[:, bass.ds(b * CH, CH)]).then_inc(copied, 1)

                    def turn(b, k8, more=True):
                        ready(b)
                        if more:
                            copy_idx(b + 1, (k8 + 1) % (2 * R))
                        hold(pool, copied, b + 1)
                        for c in range(CH):
                            one_batch(k8, c).then_inc(gathered[k8 % R], 16)
                    copy_idx(0, 0)
                    for b in range(2 * R):
                        turn(b, b)
                    with pool.Fori(1, (NB - 1) // (2 * R)) as g:
                        for k8 in range(2 * R):
                            turn(g * (2 * R) + k8, k8)
                    for b in range((NB - 1) // (2 * R) * 2 * R, NB):
                        turn(b, b % (2 * R), b + 1 < NB)

                def ready0(b):
                    if not isinstance(b, int) or b >= R:
                        hold(pool, a_free, b - R + 1)
                edge_rows(a_idx, a_gat, lambda k8, c: pool.indirect_dma_start(
                    xg[:, k8 % R, c, :], None, x, bass.IndirectOffsetOnAxis(ap=idx[:, k8, c:c + 1], axis=0)), ready0)

                def res(t, k, first):
                    if not first:
                        hold(pool, b_resst[k], (t - k) * 8)
                    hold(pool, b_qs, t + 1)
                    pool.tensor_tensor(rs[k], qs[k][:, 3 * D:4 * D], h0s[k], ALU.add).then_inc(b_res, 1)
                for t in range(2):
                    res(t, t, True)
                with pool.Fori(1, T // 2) as g:
                    for k in range(2):
                        res(g * 2 + k, k, False)

                for k in range(2):
                    pool.wait_ge(b_kvst[k], 16 * (T // 2))

                edge_rows(c_idx, c_gat, lambda k8, c: pool.indirect_dma_start(
                    kv[:, k8 % R, c, :], None, kvd, bass.IndirectOffsetOnAxis(ap=idx[:, k8, c:c + 1], axis=0),
                    compute_op=ALU.add), lambda b: hold(pool, c_ecopy, b + 1))

            @block.vector
            def _(dve):
                own_n = [0, 0]

                def link(ins):
                    own_n[1] += 1
                    ins.then_inc(own, 1)
                    dve.wait_ge(own, own_n[0] + own_n[1])

                V = nc.vector
                dve.wait_ge(in_small, 32)
                V.tensor_copy(d16, d32).then_inc(d16_done, 1)
                link(V.tensor_scalar(last, last, 7, None, ALU.logical_shift_right))
                dve.wait_ge(consts, 17)
                link(V.tensor_tensor(key, last, kiota, ALU.add))
                V.tensor_scalar(rel[0:1, R:R + NB], key[96:97, :], 2.0, None, ALU.add).then_inc(tab_made, 1)
                V.memset(rel[0:1, 0:R], 1).then_inc(tab_made, 1)
                V.tensor_scalar(ends, key[96:97, :], 1.0, None, ALU.add).then_inc(tab_made, 1)
                for j in range(8):
                    link(V.tensor_scalar(cmpk, key, scol[:, j:j + 1], None, ALU.is_lt))
                    link(V.tensor_reduce(cnt[:, j:j + 1], cmpk, AX.X, ALU.add))
                link(V.tensor_scalar(cnt[:, 0:4], cnt[:, 0:4], float(NB - 1), None, ALU.min))
                V.tensor_copy(tabc[:, 0, :], cnt[:, 0:4]).then_inc(tab_made, 1)
                V.tensor_tensor(tabc[:, 1, :], scol[:, 0:4], cnt[:, 0:4], ALU.subtract).then_inc(tab_made, 1)
                dve.wait_ge(tab_made, 5)
                link(V.tensor_scalar(cnt, cnt, float(NB - R), None, ALU.min))
                V.tensor_tensor(tabc[:, 2, :], cnt[:, 0:4], cnt[:, 4:8], ALU.subtract).then_inc(tab_made, 1)
                V.memset(tabc[:, 3, :], 0).then_inc(tab_made, 1)
                link(V.tensor_reduce(endc[:, :], endb[:, :], AX.X, ALU.add))
                V.tensor_scalar(blkbig[:, :], blk[:, :], BIG, None, ALU.mult).then_inc(own, 1)
                own_n[1] += 1
                dve.wait_ge(in_dn, 32)
                link(V.tensor_tensor(islast[:, :], dE, dN, ALU.not_equal))
                link(V.tensor_scalar(islast[:, :], islast[:, :], endc[:, 0:1], None, ALU.max))
                V.memset(fm[:, 0:1], 0.0).then_inc(own, 1)
                own_n[1] += 1
                dve.wait_ge(tab_loaded, 48)

                def cmp0(s, k, b, t):
                    dve.wait_ge(a_dst, b + 1)
                    if not isinstance(s, int) or s >= 2:
                        dve.wait_ge(a_tr, s - 1)
                    V.tensor_scalar(ST[:, k % 2, :], flat(dstb[:, bass.ds(b % R, 1), :]), tbase[:, bass.ds(t, 1)],
                                    None, ALU.is_equal).then_inc(a_cmp, 1)

                def runs(s):
                    f = fm[:, bass.ds(s * 26 + 1, 26)]
                    link(V.tensor_tensor(f, dT[:, bass.ds(s * 26 + 1, 26)], dT[:, bass.ds(s * 26, 26)], ALU.not_equal))
                    link(V.tensor_scalar(f, f, -BIG, None, ALU.mult))

                def fold0(s, k, t):
                    dve.wait_ge(a_agg, s + 1)
                    a = rowv(agg0, t)
                    V.tensor_tensor(a, a, psA[k % 2][:, 0:D], ALU.add).then_inc(a_acc, 1)
                    dve.wait_ge(a_acc, s + 1)
                vb, vt = entries(dve, 0, 0, 6), entries(dve, 1, 0, 6)
                for s in range(2):
                    cmp0(s, s, vb[s], vt[s])
                dve.wait_ge(twice_x, 1)
                dve.wait_ge(in_dt, 16)
                for s in range(4):
                    cmp0(s + 2, s + 2, vb[s + 2], vt[s + 2])
                    runs(s)
                    fold0(s, s, vt[s])
                c0, body = own_n[1], 4 * 2
                with dve.Fori(1, STEPS // 4 - 1) as g:
                    own_n[:] = [(g - 1) * body, c0]
                    vb, vt = entries(dve, 0, g * 4 + 2, 4), entries(dve, 1, g * 4, 6)
                    for k in range(4):
                        cmp0(g * 4 + k + 2, k + 2, vb[k], vt[k + 2])
                        runs(g * 4 + k)
                        fold0(g * 4 + k, k, vt[k])
                own_n[:] = [0, c0 + body * (STEPS // 4 - 2)]
                vb, vt = entries(dve, 0, STEPS - 4, 4), entries(dve, 1, STEPS - 4, 4)
                for k in range(4):
                    if k < 2:
                        cmp0(STEPS - 2 + k, k, vb[k + 2], vt[k + 2])
                    runs(STEPS - 4 + k)
                    fold0(STEPS - 4 + k, k, vt[k])

                def stats(src, t):
                    return V.bn_stats(flat(st[:, bass.ds(t, 1), :]), rowv(src, t))

                def scales(n):
                    v, sh, w = lnv[:, 0, :], lnv[:, 1, :], lnv[:, 2, :]
                    V.tensor_tensor(sh, st[:, :, 1], st[:, :, 4], ALU.add).then_inc(own, 1)
                    own_n[1] += 1
                    link(V.tensor_tensor(w, st[:, :, 1], st[:, :, 4], ALU.subtract))
                    link(V.tensor_tensor(w, w, w, ALU.mult))
                    V.tensor_scalar(w, w, 0.25, None, ALU.mult).then_inc(own, 1)
                    own_n[1] += 1
                    link(V.tensor_tensor(v, st[:, :, 2], st[:, :, 5], ALU.add))
                    V.scalar_tensor_tensor(v, v, 1.0 / D, w, ALU.mult, ALU.add).then_inc(ln_var, 1)
                    dve.wait_ge(ln_std, n)
                    link(V.reciprocal(v, v))
                    V.scalar_tensor_tensor(sh, sh, -0.5, v, ALU.mult, ALU.mult).then_inc(ln_done, 1)
                    dve.wait_ge(ln_done, n)

                def all_stats(src):
                    c = own_n[1]
                    with dve.Fori(0, T // MG) as g:
                        for k in range(MG):
                            stats(src, g * MG + k).then_inc(own, 1)
                    own_n[1] = c + T
                    dve.wait_ge(own, own_n[0] + own_n[1])
                all_stats(agg0)
                scales(1)

                def dense(t, k, first):
                    dve.wait_ge(b_mm, t + 1)
                    if not first:
                        dve.wait_ge(b_kvst[k], (t - k) * 8)
                        dve.wait_ge(b_res, t - 1)
                    V.tensor_tensor(qs[k], psW[k][:, :], ball_s, ALU.add).then_inc(b_qs, 1)
                    dve.wait_ge(b_qs, t + 1)
                    q = qs[k][:, 0:D]
                    part = [q3[:, bass.ds(t, 1), i * D:(i + 1) * D].rearrange("p a d -> p (a d)") for i in range(3)]
                    link(V.tensor_scalar(part[0], q, 0.25, None, ALU.mult))
                    link(V.scalar_tensor_tensor(rr, q, 0.25, part[0], ALU.mult, ALU.subtract))
                    link(V.tensor_copy(part[1], rr))
                    V.tensor_tensor(part[2], rr, part[1], ALU.subtract).then_inc(b_q3, 1)
                dve.wait_ge(in_b, 48)
                for t in range(2):
                    dense(t, t, True)
                c0, body = own_n[1], 2 * 3
                with dve.Fori(1, T // 2) as g:
                    own_n[:] = [(g - 1) * body, c0]
                    for k in range(2):
                        dense(g * 2 + k, k, False)
                own_n[:] = [0, c0 + body * (T // 2 - 1)]

                def cmp1(s, k, b, t):
                    dve.wait_ge(c_dst, b + 1)
                    V.tensor_scalar(ST[:, k % 2, :], flat(dstb[:, bass.ds(b % R, 1), :]), tbase[:, bass.ds(t, 1)],
                                    None, ALU.is_equal).then_inc(c_cmp, 1)

                def dots(s, k, b, kept):
                    dve.wait_ge(c_kv, b + 1)
                    dve.wait_ge(c_q, s + 1)
                    ke = kv[:, bass.ds(b % R, 1), :, 0:D].rearrange("p a c w -> p (a c) w")
                    link(V.tensor_tensor(prod.rearrange("p (c w) -> p c w", c=CH), ke,
                                         psQ[k % 2][:, :].rearrange("p (c w) -> p c w", c=CH), ALU.mult))
                    if kept is not None:
                        keep(kept)
                    link(V.tensor_reduce(lg[:, k % 2, :], prod.rearrange("p (g j) -> p g j", j=C), AX.X, ALU.add))

                def scans(s, k, b):
                    tT, f, g_, m, m1, wr = [sc4[:, i, :] for i in range(6)]
                    w = [fm[:, bass.ds(b * BLK + o, BLK)] for o in range(2)]
                    V.tensor_copy(wr[:, ::-1], w[1]).then_inc(own, 1)
                    own_n[1] += 1
                    link(V.transpose(tT, lg[:, k % 2, :]))
                    link(V.tensor_tensor_scan(f, w[0], tT, -BIG, ALU.add, ALU.max))
                    link(V.tensor_tensor_scan(g_[:, ::-1], wr, f[:, ::-1], -BIG, ALU.add, ALU.max))
                    link(V.transpose(m, g_))
                    il = islast[:, bass.ds(b * CH, CH)]
                    V.tensor_tensor(pz[:, :, :], il.unsqueeze(2).broadcast_to([P, CH, NBLK]),
                                    blkbig[:, :].unsqueeze(1).broadcast_to([P, CH, NBLK]), ALU.mult).then_inc(own, 1)
                    own_n[1] += 1
                    link(V.tensor_tensor(m1.rearrange("p (c h) -> p c h", c=CH), m.rearrange("p (c h) -> p c h", c=CH),
                                         il.unsqueeze(2).broadcast_to([P, CH, H]), ALU.mult))
                    link(V.tensor_copy(mp[:, 0, :], m1))
                    link(V.tensor_tensor(mp[:, 1, :], m1, mp[:, 0, :], ALU.subtract))
                    m8 = mp[:, :, :].rearrange("p a (c h) -> p (a c) h", c=CH)
                    V.tensor_tensor(Z[:, :, :, :, :].rearrange("p a c b h -> p (a c) b h"),
                                    m8.unsqueeze(2).broadcast_to([P, 2 * CH, NBLK, H]),
                                    blk[:, :].unsqueeze(1).unsqueeze(3).broadcast_to([P, 2 * CH, NBLK, H]),
                                    ALU.mult).then_inc(c_z, 1)

                def maxima(s, k, t):
                    dve.wait_ge(c_zmm, s + 1)
                    link(V.tensor_reduce(mx[:, :], psZ[:, 0:P].rearrange("p (b h) -> p h b", h=H), AX.X, ALU.max))
                    M = rowv(Mr, t)
                    link(V.tensor_tensor(nw[:, :], mx[:, :], M, ALU.max))
                    link(V.tensor_copy(rp[:, 0, :], nw[:, :]))
                    V.tensor_tensor(rp[:, 1, :], nw[:, :], rp[:, 0, :], ALU.subtract).then_inc(c_r, 1)
                    V.tensor_tensor(dl[:, k % 2, :], M, nw[:, :], ALU.subtract).then_inc(c_dl, 1)

                def keep(t):
                    V.tensor_tensor(rowv(Mr, t), mx[:, :], rowv(Mr, t), ALU.max).then_inc(own, 1)
                    own_n[1] += 1

                def shifts(s, k):
                    dve.wait_ge(c_rexp, s + 1)
                    V.tensor_tensor(dd[:, :], lg[:, k % 2, :], psR[:, 0:CH * H], ALU.subtract).then_inc(c_d, 1)

                def weigh(s, b):
                    dve.wait_ge(c_ex, s + 1)
                    v4 = kv[:, bass.ds(b % R, 1), :, D:2 * D].rearrange("p a c (h j) -> p (a c) h j", h=H)
                    V.tensor_tensor(wvx[:, :, :, 0:C], v4, wvx[:, :, :, C:C + 1].broadcast_to([P, CH, H, C]),
                                    ALU.mult).then_inc(c_wv, 1)

                def fold1(s, k, t):
                    dve.wait_ge(c_agg, s + 1)
                    dve.wait_ge(c_sc, s + 1)
                    a = rowv(agg1, t)
                    a3 = a.rearrange("p (h j) -> p h j", h=H)
                    link(V.tensor_tensor(a3, a3, scl[:, k % 2, :].unsqueeze(2).broadcast_to([P, H, C + 1]), ALU.mult))
                    V.tensor_tensor(a, a, psA[k % 2][:, 0:AW], ALU.add).then_inc(c_acc, 1)
                    dve.wait_ge(c_acc, s + 1)

                PER = 2 + 9 + 4 + 1
                def iteration(s, k, b, t, first=9, more=True):
                    if first >= 1:
                        maxima(s - 1, k - 1, t[1])
                    dots(s, k, b[2], t[1] if first >= 1 else None)
                    if first >= 1:
                        shifts(s - 1, k - 1)
                    if more:
                        cmp1(s + 1, k + 1, b[3], t[3])
                    scans(s, k, b[2])
                    if first >= 1:
                        weigh(s - 1, b[1])
                    if first >= 2:
                        fold1(s - 2, k - 2, t[0])

                vb, vt = entries(dve, 0, 0, 5), entries(dve, 1, 0, 5)
                dve.wait_ge(b_q3, T)
                V.memset(Mr[:, :, :], -BIG).then_inc(own, 1)
                own_n[1] += 1
                V.memset(work[:, :], 0.0).then_inc(c_wv, 1)
                for k in range(2):
                    dve.wait_ge(b_h0st[k], 8 * T)
                dve.wait_ge(b_res, T)
                V.memset(big1[:, :], 0.0).then_inc(own, 1)
                own_n[1] += 1
                dve.wait_ge(own, own_n[0] + own_n[1])
                cmp1(0, 0, vb[0], vt[0])
                for s in range(4):
                    iteration(s, s, [None, None if s < 1 else vb[s - 1], vb[s], vb[s + 1]],
                              [None if s < 2 else vt[s - 2], None if s < 1 else vt[s - 1], vt[s], vt[s + 1]], s)
                c0, body = own_n[1], 4 * PER
                with dve.Fori(1, STEPS // 4 - 1) as g:
                    own_n[:] = [(g - 1) * body, c0]
                    vb, vt = entries(dve, 0, g * 4 - 2, 7), entries(dve, 1, g * 4 - 2, 7)
                    for k in range(4):
                        iteration(g * 4 + k, k, vb[k:k + 4], vt[k:k + 4])
                    assert own_n[1] - c0 == body, own_n[1] - c0
                own_n[:] = [0, c0 + body * (STEPS // 4 - 2)]
                vb, vt = entries(dve, 0, STEPS - 6, 6) + (None,), entries(dve, 1, STEPS - 6, 6) + (None,)
                for k in range(4):
                    iteration(STEPS - 4 + k, k, vb[k:k + 4], vt[k:k + 4], 9, k < 3)
                maxima(STEPS - 1, 3, vt[5])
                shifts(STEPS - 1, 3)
                weigh(STEPS - 1, vb[5])
                fold1(STEPS - 2, 2, vt[4])
                fold1(STEPS - 1, 3, vt[5])

                tiny = 1e-30
                link(V.tensor_scalar(rd, agg1.rearrange("p t (h j) -> p t h j", h=H)[:, :, :, C], tiny, None, ALU.add))
                link(V.reciprocal(rd, rd))

                def y1(m, k, g):
                    rows_ = bass.ds(m * MG, MG)
                    y = Y[:, rows_, :].rearrange("p t (h j) -> p (t h) j", h=H)
                    a = agg1[:, rows_, :].rearrange("p t (h j) -> p (t h) j", h=H)[:, :, 0:C]
                    r = rd[:, rows_, :].rearrange("p t h -> p (t h)").unsqueeze(2).broadcast_to([P, MG * H, C])
                    link(V.tensor_tensor(y, a, r, ALU.mult))
                    dve.wait_ge(d_res[k], g * 16 + 16)
                    yf = Y[:, rows_, :].rearrange("p t d -> p (t d)")
                    V.tensor_tensor(yf, yf, resb[k], ALU.add).then_inc(d_y, 1)
                    dve.wait_ge(d_y, m + 1)
                    for i in range(MG):
                        stats(Y, m * MG + i).then_inc(own, 1)
                c0 = own_n[1]
                with dve.Fori(0, T // MG // 2) as g:
                    own_n[:] = [g * 2 * (MG + 1), c0]
                    for k in range(2):
                        y1(g * 2 + k, k, g)
                        own_n[1] += MG
                own_n[:] = [0, c0 + T // MG * (MG + 1)]
                dve.wait_ge(own, own_n[1])
                scales(2)

                def pair_rows(m):
                    return Y[:, bass.ds(m * 2, 2), :]

                def h_rows(m, k):
                    dve.wait_ge(d_hn, m + 1)
                    y = pair_rows(m)
                    link(V.tensor_tensor(y, y, g1_s.unsqueeze(1).broadcast_to([P, 2, D]), ALU.mult))
                    V.tensor_tensor(hs[k], y, b1_s.unsqueeze(1).broadcast_to([P, 2, D]), ALU.add).then_inc(d_h, 1)

                def y2(m, k):
                    y = pair_rows(m)
                    dve.wait_ge(d_ht, m + 1)
                    link(V.tensor_tensor(y, hs[k], bf2_s.unsqueeze(1).broadcast_to([P, 2, D]), ALU.add))
                    dve.wait_ge(d_f2, m + 1)
                    V.tensor_tensor(flat(y), flat(y), psF2[k][:, 0:2 * D], ALU.add).then_inc(d_y2, 1)
                    dve.wait_ge(d_y2, m + 1)
                    for i in range(2):
                        stats(Y, m * 2 + i).then_inc(own, 1)
                    own_n[1] += 2
                dve.wait_ge(in_d, 64)
                h_rows(0, 0)
                h_rows(1, 1)
                c0, body = own_n[1], 2 * 4
                with dve.Fori(0, T // 4 - 1) as g:
                    own_n[:] = [g * body, c0]
                    for k in range(2):
                        y2(g * 2 + k, k)
                        h_rows(g * 2 + k + 2, k)
                    assert own_n[1] - c0 == body
                own_n[:] = [0, c0 + body * (T // 4 - 1)]
                y2(T // 2 - 3, 0)
                h_rows(T // 2 - 1, 0)
                y2(T // 2 - 2, 1)
                y2(T // 2 - 1, 0)
                dve.wait_ge(own, own_n[1])
                scales(3)

                def u_rows(m, k, g):
                    rows_ = bass.ds(m * MG, MG)
                    y = Y[:, rows_, :]
                    dve.wait_ge(d_n2, m + 1)
                    link(V.tensor_tensor(y, y, g2_s.unsqueeze(1).broadcast_to([P, MG, D]), ALU.mult))
                    link(V.tensor_tensor(y, y, b2_s.unsqueeze(1).broadcast_to([P, MG, D]), ALU.add))
                    dve.wait_ge(d_h0[k], g * 16 + 16)
                    V.tensor_tensor(flat(y), flat(y), h0b[k], ALU.add).then_inc(d_u, 1)
                    dve.wait_ge(d_u, m + 1)
                    for i in range(MG):
                        stats(Y, m * MG + i).then_inc(own, 1)
                    own_n[1] += MG
                c0 = own_n[1]
                with dve.Fori(0, T // MG // 2) as g:
                    own_n[:] = [g * 2 * (MG + 2), c0]
                    for k in range(2):
                        u_rows(g * 2 + k, k, g)
                own_n[:] = [0, c0 + T // MG * (MG + 2)]
                dve.wait_ge(own, own_n[1])
                scales(4)

            @block.tensor
            def _(pe):
                M = nc.tensor.matmul
                chunk = lambda a, k, c: a[:, k % 2, c * P:(c + 1) * P]
                pe.wait_ge(consts, 17)
                pe.wait_ge(tab_loaded, 48)

                def turn_rows0(s, k):
                    pe.wait_ge(a_cmp, s + 1)
                    if not isinstance(s, int) or s >= 1:
                        pe.wait_ge(a_s32, s)
                    for c in range(CH):
                        last_ = nc.tensor.transpose(psS[:, c * P:(c + 1) * P], chunk(ST, k, c), ident[:, :])
                    last_.then_inc(a_tr, 1)

                def agg_0(s, k, b):
                    pe.wait_ge(a_s32, s + 1)
                    hold(pe, a_x, b + 1)
                    if not isinstance(s, int) or s >= 2:
                        hold(pe, a_acc, s - 1)
                    for c in range(CH):
                        last_ = M(psA[k % 2][:, 0:D], chunk(S32, k, c), flat(xg[:, bass.ds(b % R, 1), c, :]),
                                  start=(c == 0), stop=(c == CH - 1))
                    last_.then_inc(a_agg, 1)
                vb = entries(pe, 0, 0, 4)
                turn_rows0(0, 0)
                for s in range(4):
                    turn_rows0(s + 1, s + 1)
                    agg_0(s, s, vb[s])
                with pe.Fori(1, STEPS // 4 - 1) as g:
                    vb = entries(pe, 0, g * 4, 4)
                    for k in range(4):
                        turn_rows0(g * 4 + k + 1, k + 1)
                        agg_0(g * 4 + k, k, vb[k])
                vb = entries(pe, 0, STEPS - 4, 4)
                for k in range(4):
                    if k < 3:
                        turn_rows0(STEPS - 3 + k, k + 1)
                    agg_0(STEPS - 4 + k, k, vb[k])

                def turn_h0(t, k, first=False):
                    hold(pe, b_h0, t + 1)
                    if not first:
                        hold(pe, b_ht, t - 1)
                    nc.tensor.transpose(psT[k % 2][:, 0:P], h0s[k % 2], identf[:, :]).then_inc(b_tr, 1)

                def project(t, k, first=False):
                    pe.wait_ge(b_ht, t + 1)
                    if not first:
                        pe.wait_ge(b_qs, t - 1)
                    M(psW[k][:, :], hT[k], wall_s, start=True, stop=True).then_inc(b_mm, 1)
                pe.wait_ge(in_b, 48)
                turn_h0(0, 0, True)
                turn_h0(1, 1, True)
                project(0, 0, True)
                turn_h0(2, 0)
                project(1, 1, True)
                with pe.Fori(1, T // 2 - 1) as g:
                    for k in range(2):
                        turn_h0(g * 2 + k + 1, k + 1)
                        project(g * 2 + k, k)
                turn_h0(T - 1, 1)
                project(T - 2, 0)
                project(T - 1, 1)

                def edge_e(b):
                    if isinstance(b, int) and b >= 1 or not isinstance(b, int):
                        hold(pe, c_ecopy, b)
                    hold(pe, c_attr, b + 1)
                    for c in range(CH):
                        last_ = M(psE[:, c * D:(c + 1) * D], attr[:, c * P:(c + 1) * P], we_s[:, :], start=True, stop=True)
                    last_.then_inc(c_e, 1)

                def q_rows(s, k, t):
                    hold(pe, c_cmp, s + 1)
                    for c in range(CH):
                        for i in range(3):
                            w = q3[:, bass.ds(t, 1), i * D:(i + 1) * D].rearrange("p a d -> p (a d)")
                            last_ = M(psQ[k % 2][:, c * D:(c + 1) * D], chunk(ST, k, c), w, start=(i == 0), stop=(i == 2))
                    last_.then_inc(c_q, 1)
                    if not isinstance(s, int) or s >= 1:
                        pe.wait_ge(c_sb, s)
                    for c in range(CH):
                        last_ = nc.tensor.transpose(psS[:, c * P:(c + 1) * P], chunk(ST, k, c), ident[:, :])
                    last_.then_inc(c_tr, 1)

                def block_maxima(s, k):
                    pe.wait_ge(c_z, s + 1)
                    M(psZ[:, 0:P], ones[:, :], neg[:, :], start=True, stop=False)
                    pe.wait_ge(c_sb, s + 1)
                    for c in range(CH):
                        o = psZ[:, c * NBLK * H:(c + 1) * NBLK * H]
                        M(o, chunk(Sb, k, c), pz[:, c, :].unsqueeze(2).broadcast_to([P, NBLK, H]), start=False, stop=False)
                        M(o, chunk(Sb, k, c), Z[:, 0, c, :, :].rearrange("p b h -> p (b h)"), start=False, stop=False)
                        last_ = M(o, chunk(Sb, k, c), Z[:, 1, c, :, :].rearrange("p b h -> p (b h)"),
                                  start=False, stop=(c == CH - 1))
                    last_.then_inc(c_zmm, 1)

                def expand(s, k):
                    pe.wait_ge(c_r, s + 1)
                    for c in range(CH):
                        for i in range(2):
                            last_ = M(psR[:, c * H:(c + 1) * H], chunk(ST, k, c), rp[:, i, :], start=(i == 0), stop=(i == 1))
                    last_.then_inc(c_rexp, 1)

                def agg_1(s, k):
                    pe.wait_ge(c_wv, s + 2)
                    pe.wait_ge(c_s32, s + 1)
                    for c in range(CH):
                        last_ = M(psA[k % 2][:, 0:AW], chunk(S32, k, c), work[:, 512 + c * AW:512 + (c + 1) * AW],
                                  start=(c == 0), stop=(c == CH - 1))
                    last_.then_inc(c_agg, 1)

                def iteration(s, k, b, new, tn, first=9, more=True):
                    if first >= 1:
                        expand(s - 1, k - 1)
                    if more:
                        q_rows(s + 1, k + 1, tn)
                    with pe.If(new):
                        edge_e(b + (R - 1))
                    block_maxima(s, k)
                    if first >= 1:
                        agg_1(s - 1, k - 1)
                for b in range(R):
                    edge_e(b)
                vb, vn, vt = entries(pe, 0, 0, 4), entries(pe, 2, 0, 4), entries(pe, 1, 0, 5)
                pe.wait_ge(b_q3, T)
                q_rows(0, 0, vt[0])
                for s in range(4):
                    iteration(s, s, vb[s], vn[s], vt[s + 1], s)
                with pe.Fori(1, STEPS // 4 - 1) as g:
                    vb, vn, vt = entries(pe, 0, g * 4, 4), entries(pe, 2, g * 4, 4), entries(pe, 1, g * 4 + 1, 4)
                    for k in range(4):
                        iteration(g * 4 + k, k, vb[k], vn[k], vt[k])
                vb, vn, vt = entries(pe, 0, STEPS - 4, 4), entries(pe, 2, STEPS - 4, 4), entries(pe, 1, STEPS - 3, 3)
                for k in range(4):
                    iteration(STEPS - 4 + k, k, vb[k], vn[k], vt[k] if k < 3 else None, 9, k < 3)
                expand(STEPS - 1, 3)
                agg_1(STEPS - 1, 3)

                def turn_h(m, k, first=False):
                    hold(pe, d_h, m + 1)
                    if not first:
                        hold(pe, d_ht, m - 1)
                    for i in range(2):
                        last_ = nc.tensor.transpose(psT2[k][:, i * P:(i + 1) * P], hs[k][:, i, :], identf[:, :])
                    last_.then_inc(d_tr, 1)

                def ffn1(m, k, first=False):
                    pe.wait_ge(d_ht, m + 1)
                    if not first:
                        pe.wait_ge(d_g, m * 4 - 4)
                    for c in range(4):
                        last_ = M(psF1[k][c // 2][:, c % 2 * 256:c % 2 * 256 + 256], wf1_s[:, c * P:(c + 1) * P], hT2[k],
                                  start=True, stop=True)
                        if c % 2:
                            last_.then_inc(d_f1, 1)

                def ffn2(m, k, first=False):
                    pe.wait_ge(d_g, m * 4 + 4)
                    if not first:
                        pe.wait_ge(d_y2, m - 1)
                    for i in range(2):
                        for c in range(4):
                            last_ = M(psF2[k][:, i * P:(i + 1) * P], gT[k][:, c, i * P:(i + 1) * P],
                                      wf2_s[:, c * P:(c + 1) * P], start=(c == 0), stop=(c == 3))
                    last_.then_inc(d_f2, 1)
                pe.wait_ge(in_d, 64)
                turn_h(0, 0, True)
                turn_h(1, 1, True)
                ffn1(0, 0, True)
                ffn1(1, 1, True)
                ffn2(0, 0, True)
                turn_h(2, 0)
                ffn1(2, 0)
                ffn2(1, 1, True)
                with pe.Fori(1, T // 4) as g:
                    for k in range(2):
                        turn_h(g * 2 + k + 1, (k + 1) % 2)
                        ffn1(g * 2 + k + 1, (k + 1) % 2)
                        ffn2(g * 2 + k, k)
                ffn2(T // 2 - 1, 0)

            @block.scalar
            def _(act):
                A = nc.scalar.activation
                act.wait_ge(in_x, 16)
                A(flat(agg0), flat(agg0), ACT.Copy, scale=2.0).then_inc(twice_x, 1)

                def rows0(s, k):
                    act.wait_ge(a_tr, s + 1)
                    if not isinstance(s, int) or s >= 2:
                        act.wait_ge(a_agg, s - 1)
                    A(S32[:, k % 2, :], psS, ACT.Copy).then_inc(a_s32, 1)
                for s in range(4):
                    rows0(s, s)
                with act.Fori(1, STEPS // 4) as g:
                    for k in range(4):
                        rows0(g * 4 + k, k)

                def std(n):
                    act.wait_ge(ln_var, n)
                    A(lnv[:, 0, :], lnv[:, 0, :], ACT.Sqrt, bias=epsc[:, 0:1]).then_inc(ln_std, 1)

                def norm(src, t):
                    return A(rowv(src, t), rowv(src, t), ACT.Identity, scale=lnv[:, 0, bass.ds(t, 1)], bias=lnv[:, 1, bass.ds(t, 1)])
                std(1)
                act.wait_ge(ln_done, 1)

                def copy_hT(t, k, first=False):
                    act.wait_ge(b_tr, t + 1)
                    if not first:
                        act.wait_ge(b_mm, t - 1)
                    A(hT[k], psT[k][:, 0:P], ACT.Copy).then_inc(b_ht, 1)
                def norm0(t, k, first=False):
                    if not first:
                        hold(act, b_h0st[k], (t - k) * 8)
                        hold(act, b_res, t - 1)
                    A(h0s[k], rowv(agg0, t), ACT.Identity, scale=lnv[:, 0, bass.ds(t, 1)],
                      bias=lnv[:, 1, bass.ds(t, 1)]).then_inc(b_h0, 1)
                norm0(0, 0, True)
                norm0(1, 1, True)
                copy_hT(0, 0, True)
                norm0(2, 0)
                copy_hT(1, 1, True)
                with act.Fori(1, T // 2 - 1) as g:
                    for k in range(2):
                        norm0(g * 2 + k + 1, (k + 1) % 2)
                        copy_hT(g * 2 + k, k)
                norm0(T - 1, 1)
                copy_hT(T - 2, 0)
                copy_hT(T - 1, 1)

                def copy_e(b):
                    free = act.value_load(rel[0:1, bass.ds(b, 1)], min_val=1, max_val=STEPS + 1)
                    hold(act, c_wv, free)
                    hold(act, c_e, b + 1)
                    dst = kv[:, bass.ds(b % R, 1), :, :].rearrange("p a c (w d) -> p (a c) w d", w=2)
                    src = psE[:, :].rearrange("p (c d) -> p c d", c=CH).unsqueeze(2).broadcast_to([P, CH, 2, D])
                    A(dst, src, ACT.Copy).then_inc(c_ecopy, 1)

                def rescale(s, k):
                    act.wait_ge(c_dl, s + 1)
                    A(scl[:, k % 2, :], dl[:, k % 2, :], ACT.Exp).then_inc(c_sc, 1)

                def weights(s, first=False):
                    act.wait_ge(c_d, s + 1)
                    if not first:
                        act.wait_ge(c_agg, s)
                    A(wvx[:, :, :, C], dd[:, :].rearrange("p (c h) -> p c h", c=CH), ACT.Exp).then_inc(c_ex, 1)

                def rows_bf(s, k):
                    act.wait_ge(c_tr, s + 1)
                    if not isinstance(s, int) or s >= 2:
                        act.wait_ge(c_zmm, s - 1)
                    A(Sb[:, k % 2, :], psS, ACT.Copy).then_inc(c_sb, 1)

                def rows_f(s, k):
                    act.wait_ge(c_sb, s + 1)
                    if not isinstance(s, int) or s >= 2:
                        act.wait_ge(c_agg, s - 1)
                    A(S32[:, k % 2, :], Sb[:, k % 2, :], ACT.Copy).then_inc(c_s32, 1)

                def iteration(s, k, b, new, first=9, more=True):
                    if first >= 1:
                        rescale(s - 1, k - 1)
                    rows_f(s, k)
                    if first >= 1:
                        weights(s - 1, first == 1)
                    if more:
                        rows_bf(s + 1, k + 1)
                    with act.If(new):
                        copy_e(b + (R - 1))
                for k in range(2):
                    act.wait_ge(b_kvst[k], 16 * (T // 2))
                    act.wait_ge(b_resst[k], 16 * (T // 2))
                act.wait_ge(b_q3, T)
                for b in range(R):
                    copy_e(b)
                rows_bf(0, 0)
                vb, vn = entries(act, 0, 0, 4), entries(act, 2, 0, 4)
                for s in range(4):
                    iteration(s, s, vb[s], vn[s], s)
                with act.Fori(1, STEPS // 4 - 1) as g:
                    vb, vn = entries(act, 0, g * 4, 4), entries(act, 2, g * 4, 4)
                    for k in range(4):
                        iteration(g * 4 + k, k, vb[k], vn[k])
                vb, vn = entries(act, 0, STEPS - 4, 4), entries(act, 2, STEPS - 4, 4)
                for k in range(4):
                    iteration(STEPS - 4 + k, k, vb[k], vn[k], 9, k < 3)
                rescale(STEPS - 1, 3)
                weights(STEPS - 1)
                std(2)
                act.wait_ge(ln_done, 2)

                def norm_pair(m):
                    for i in range(2):
                        last_ = norm(Y, m * 2 + i)
                    last_.then_inc(d_hn, 1)

                def copy_hT2(m, k, first=False):
                    act.wait_ge(d_tr, m + 1)
                    if not first:
                        act.wait_ge(d_f1, m * 2 - 2)
                    A(hT2[k], psT2[k][:, 0:2 * P], ACT.Copy).then_inc(d_ht, 1)

                def gelu(m, k, first=False):
                    if not first:
                        act.wait_ge(d_f2, m - 1)
                    for c in range(4):
                        if c % 2 == 0:
                            act.wait_ge(d_f1, m * 2 + c // 2 + 1)
                        A(gT[k][:, c, :], psF1[k][c // 2][:, c % 2 * 256:c % 2 * 256 + 256], ACT.Gelu,
                          bias=bf1_s[:, c:c + 1]).then_inc(d_g, 1)
                act.wait_ge(in_d, 64)
                for m in range(3):
                    norm_pair(m)
                copy_hT2(0, 0, True)
                copy_hT2(1, 1, True)
                gelu(0, 0, True)
                copy_hT2(2, 0)
                gelu(1, 1, True)
                with act.Fori(1, T // 4) as g:
                    for k in range(2):
                        norm_pair(g * 2 + k + 1)
                        copy_hT2(g * 2 + k + 1, (k + 1) % 2)
                        gelu(g * 2 + k, k)
                gelu(T // 2 - 1, 0)
                std(3)
                act.wait_ge(ln_done, 3)
                with act.Fori(0, T // MG) as m:
                    for i in range(MG):
                        last_ = norm(Y, m * MG + i)
                    last_.then_inc(d_n2, 1)
                std(4)
                act.wait_ge(ln_done, 4)
                with act.Fori(0, T // MG) as m:
                    for i in range(MG):
                        last_ = norm(Y, m * MG + i)
                    last_.then_inc(d_o, 1)


def kernel(x, src, dst, edge_attr_64, L1_gnn_Wq, L1_gnn_bq, L1_gnn_Wk, L1_gnn_bk, L1_gnn_Wv, L1_gnn_bv, L1_gnn_We,
           L1_gnn_Wskip, L1_gnn_bskip, L1_gnn_g1, L1_gnn_b1, L1_gnn_g2, L1_gnn_b2, L1_gnn_Wf1, L1_gnn_bf1, L1_gnn_Wf2,
           L1_gnn_bf2):
    import numpy as np
    import concourse.bacc as bacc
    from concourse.bass_utils import run_bass_kernel_spmd as run
    cont = np.ascontiguousarray
    x, src, dst, ea = (np.asarray(a) for a in (x, src, dst, edge_attr_64))
    srcp = np.concatenate([src, np.zeros(EPAD - E, src.dtype)])
    dstp = np.concatenate([dst, np.full(EPAD - E, NPAD - 1, dst.dtype)])
    eap = np.concatenate([ea, np.zeros((EPAD - E, ED), ea.dtype)])
    blocks = dstp.reshape(NB, CH, NBLK, BLK).transpose(2, 1, 0, 3)
    dstt = np.repeat(blocks, H, axis=1).reshape(P, NB * BLK)
    width = 26 * STEPS + 1
    dstt = np.concatenate([dstt, np.full((P, width - dstt.shape[1]), NPAD - 1, dst.dtype)], axis=1)
    nxt = np.concatenate([dstp[1:], dstp[-1:]])
    bycol = lambda a: cont(a.reshape(NB * CH, P).T)
    arrays = {
        "x": np.concatenate([x, np.zeros((NPAD - N, D), x.dtype)]),
        "srcl": bycol(srcp), "dstrow": dstp.reshape(P, EPAD // P), "dstt": cont(dstt),
        "dste": bycol(dstp), "dstn": bycol(nxt), "lastd": cont(dstp[BE - 1::BE][None, :]),
        "attrt": cont(eap.T),
        "wall": np.concatenate([L1_gnn_Wq, L1_gnn_Wk, L1_gnn_Wv, L1_gnn_Wskip], axis=1),
        "ball": np.concatenate([L1_gnn_bq, L1_gnn_bk, L1_gnn_bv, L1_gnn_bskip])[None, :],
        "we": cont(L1_gnn_We), "wf1": cont(L1_gnn_Wf1), "wf2": cont(L1_gnn_Wf2),
        "rows": np.concatenate([L1_gnn_g1, L1_gnn_b1, L1_gnn_g2, L1_gnn_b2, L1_gnn_bf2])[None, :],
        "bf1": cont(np.asarray(L1_gnn_bf1).reshape(4, P).T),
    }
    nc = bacc.Bacc("TRN2", target_bir_lowering=False, num_devices=1)
    aps = [nc.dram_tensor(k, v.shape, mybir.dt.from_np(v.dtype), kind="ExternalInput").ap() for k, v in arrays.items()]
    out = nc.dram_tensor("out", (NPAD, D), f32, kind="ExternalOutput").ap()
    build(nc, *aps, out)
    r = run(nc, [arrays], core_ids=[0])
    return r.results[0]["out"][:N]
```
